# Optimizing a Trainium2 kernel written in Bass

```python
import numpy as np
import jax
import jax.numpy as jnp

def _softmax(x, axis=-1):
    return jax.nn.softmax(x, axis=axis)

def _gelu(x):
    return jax.nn.gelu(x, approximate=True)

def _silu(x):
    return jax.nn.silu(x)

def _sigmoid(x):
    return jax.nn.sigmoid(x)

def _layernorm(x, axis=-1, eps=1e-05):
    m = jnp.mean(x, axis=axis, keepdims=True)
    v = jnp.var(x, axis=axis, keepdims=True)
    return (x - m) / jnp.sqrt(v + eps)

def _scatter_add(tgt, idx, src, axis=0):
    return tgt.at[idx].add(src)

def _segment_sum(src, seg, n):
    return jax.ops.segment_sum(src, seg, n)
kernel_name = 'mk_rec_standalone_d1_rec_r8_7b5d07'

def setup_inputs(seed: int=0):
    np.random.seed(seed)
    _w = jnp.asarray

    def _rec_inputs():
        import jax
        import jax.numpy as jnp
        _rk = jax.random.key(seed)
        r_padded_embeddings = -0.000161372 + 0.999968 * jax.random.normal(jax.random.fold_in(_rk, 1), (512, 200, 128), jnp.float32)
        r_lengths = jax.random.randint(jax.random.fold_in(_rk, 2), (512,), 1, 200, jnp.int32)
        return (r_padded_embeddings, r_lengths)
    r_padded_embeddings, r_lengths = _rec_inputs()

    def _L0_rec_setup():
        import jax, jax.numpy as jnp
        import numpy as np
        LN_EPS = 1e-05
        key = jax.random.key(seed)
        k1, k2, k3 = jax.random.split(key, 3)
        B, L, D = (512, 200, 128)
        padded_embeddings = jax.random.normal(k1, (B, L, D), dtype=jnp.float32)
        lengths = jnp.maximum(jax.random.randint(k2, (B,), 0, L), 1).astype(jnp.int64)
        w_att = jax.random.normal(k3, (D,), dtype=jnp.float32) * (1.0 / np.sqrt(D))
        b_att = jnp.zeros((1,), dtype=jnp.float32)
        ln_gamma = jnp.ones((D,), dtype=jnp.float32)
        ln_beta = jnp.zeros((D,), dtype=jnp.float32)
        return {'padded_embeddings': padded_embeddings, 'lengths': lengths, 'w_att': w_att, 'b_att': b_att, 'ln_gamma': ln_gamma, 'ln_beta': ln_beta}
    _L0_rec_all = _L0_rec_setup()
    _L0_rec_in = {k: v for k, v in _L0_rec_all.items() if k in ('w_att', 'b_att', 'ln_gamma', 'ln_beta')}
    del _L0_rec_all
    return {'r_padded_embeddings': r_padded_embeddings, 'r_lengths': r_lengths, 'L0_rec_w_att': _L0_rec_in['w_att'], 'L0_rec_b_att': _L0_rec_in['b_att'], 'L0_rec_ln_gamma': _L0_rec_in['ln_gamma'], 'L0_rec_ln_beta': _L0_rec_in['ln_beta']}

def reference(r_padded_embeddings, r_lengths, L0_rec_w_att, L0_rec_b_att, L0_rec_ln_gamma, L0_rec_ln_beta):
    import jax
    import jax.numpy as jnp

    def _L0_rec_ref(padded_embeddings, lengths, w_att, b_att, ln_gamma, ln_beta):
        import jax, jax.numpy as jnp
        import numpy as np
        LN_EPS = 1e-05
        scores = jnp.einsum('bld,d->bl', padded_embeddings, w_att) + b_att[0]
        L = padded_embeddings.shape[1]
        mask = jnp.arange(L)[None, :] < lengths[:, None]
        scores = jnp.where(mask, scores, -jnp.inf)
        attn = jax.nn.softmax(scores, axis=-1)
        pooled = jnp.einsum('bld,bl->bd', padded_embeddings, attn)
        mu = jnp.mean(pooled, axis=-1, keepdims=True)
        var = jnp.var(pooled, axis=-1, keepdims=True)
        normed = (pooled - mu) * jax.lax.rsqrt(var + LN_EPS)
        return normed * ln_gamma + ln_beta
    y = _L0_rec_ref(r_padded_embeddings, r_lengths, L0_rec_w_att, L0_rec_b_att, L0_rec_ln_gamma, L0_rec_ln_beta)
    return y

_drawn_inputs = setup_inputs


def setup_inputs(seed=0):
    import zlib

    import numpy as np

    out = dict(_drawn_inputs(seed))
    spreads = {'L0_rec_ln_gamma': (1.0, 0.2), 'L0_rec_ln_beta': (0.0, 0.1)}
    factors = {}
    for name, (base, spread) in spreads.items():
        noise = np.random.default_rng([zlib.crc32(name.encode()), seed]).standard_normal(out[name].shape)
        drawn = base * np.exp(spread * noise) if base else spread * noise
        out[name] = jnp.asarray(drawn.astype(out[name].dtype))
    for name, factor in factors.items():
        out[name] = (out[name] * factor).astype(out[name].dtype)
    return out
```

```python
from contextlib import ExitStack

import concourse.bass as bass
from concourse import mybir

ALU = mybir.AluOpType
ACT = mybir.ActivationFunctionType
AX_X = mybir.AxisListType.X
F32 = mybir.dt.float32
I32 = mybir.dt.int32

P = 128
LN_EPS = 1e-5
MASKED = -3.0e38


def attention_pool_layernorm(nc, x, lengths, w_att, b_att, ln_gamma, ln_beta, out):
    B, L, D = x.shape
    SEGS = 8
    ROWS = L // SEGS
    TB = P // SEGS
    TILES = B // TB
    PB = 2 * TB
    GROUPS = P // PB
    SLOTS = 2 * GROUPS
    ROUNDS = TILES // SLOTS
    DVE_ROWS = 17
    POOL_ROWS = ROWS - DVE_ROWS
    assert L % SEGS == 0 and D == P and PB == 32 and TILES % SLOTS == 0

    x_tiles = x.rearrange("(t b) (s j) d -> t (b s) (j d)", b=TB, s=SEGS)
    out_rounds = out.rearrange("(g p) d -> g p d", p=P)
    len_tiles = lengths.rearrange("(t b) -> t b", b=TB)

    with ExitStack() as ctx:
        def sb(name, shape, dt=F32):
            return ctx.enter_context(nc.sbuf_tensor(name, shape, dt))

        def psum(name, shape):
            return ctx.enter_context(nc.psum_tensor(name, shape, F32))

        def sem(name):
            return ctx.enter_context(nc.semaphore(name))

        xs = [sb(f"x_slot{s}", [P, ROWS, D]) for s in range(SLOTS)]
        w_rep = sb("w_rep", [P, D])
        gamma_rep = sb("gamma_rep", [P, D])
        beta_rep = sb("beta_rep", [P, D])
        b_rep = sb("b_rep", [P, 1])
        ident = sb("ident", [P, P])
        sel = sb("sel", [P, 3 * TB])
        fold = sb("fold", [P, PB])
        len_i = sb("len_i", [TILES, TB], I32)
        len_f = sb("len_f", [TILES, TB])
        len_off = sb("len_off", [TILES, TB])
        len_end = sb("len_end", [TILES, TB])
        len_exp = sb("len_exp", [TILES, TB, SEGS])
        len_p = sb("len_p", [P, TILES])
        pos = sb("pos", [P, ROWS])
        is_pad = sb("is_pad", [P, TILES, ROWS])
        penalty = sb("penalty", [P, TILES, ROWS])
        dve_prods = sb("dve_prods", [P, 2, DVE_ROWS, D])
        prods = sb("prods", [P, 2, POOL_ROWS, D])
        scores = sb("scores", [P, 2, 2, ROWS])
        masked = sb("masked", [P, 2, 2, ROWS])
        seg_max = sb("seg_max", [P, 2, 2])
        batch_max = sb("batch_max", [2, 2, TB])
        neg_max_exp = sb("neg_max_exp", [2, 2, TB, SEGS])
        neg_max = sb("neg_max", [P, 2, 2])
        probs = sb("probs", [P, 2, 2, ROWS])
        seg_sum = sb("seg_sum", [P, 2, 2])
        weights = sb("weights", [P, 2, 2, ROWS, PB])
        partial = sb("partial", [P, 2, D])
        inv_sum = sb("inv_sum", [P, 1])
        pooled = sb("pooled", [P, ROUNDS, D])
        stats = sb("stats", [P, ROUNDS, 6])
        mean_var = sb("mean_var", [P, ROUNDS, 2])
        var_eps = sb("var_eps", [P, ROUNDS])
        std = sb("std", [P, ROUNDS])
        rstd = sb("rstd", [P, ROUNDS])
        normed = sb("normed", [P, ROUNDS, D])
        scaled = sb("scaled", [P, ROUNDS, D])
        result = sb("result", [P, ROUNDS, D])

        w_ps = psum("w_ps", [P, 512])
        len_ps = psum("len_ps", [P, 512])
        seg_max_ps = psum("seg_max_ps", [P, 512])
        neg_max_ps = psum("neg_max_ps", [P, 512])
        partial_ps = [psum(f"partial_ps{k}", [P, 512]) for k in range(2)]
        pooled_ps = psum("pooled_ps", [P, 512])

        consts_landed = sem("consts_landed")
        x_landed = [sem(f"x_landed{s}") for s in range(SLOTS)]
        tiles_summed = sem("tiles_summed")
        sel_step = sem("sel_step")
        consts_made = sem("consts_made")
        setup_dve = sem("setup_dve")
        len_exp_ready = sem("len_exp_ready")
        len_p_ready = sem("len_p_ready")
        w_ps_ready = sem("w_ps_ready")
        prods_ready = sem("prods_ready")
        dve_scores = sem("dve_scores")
        act_scores = sem("act_scores")
        masked_ready = sem("masked_ready")
        seg_max_ready = sem("seg_max_ready")
        seg_max_turned = sem("seg_max_turned")
        batch_max_ready = sem("batch_max_ready")
        neg_max_spread = sem("neg_max_spread")
        neg_max_turned = sem("neg_max_turned")
        neg_max_ready = sem("neg_max_ready")
        probs_ready = sem("probs_ready")
        weights_ready = sem("weights_ready")
        partial_copied = sem("partial_copied")
        pooled_summed = sem("pooled_summed")
        pooled_read = sem("pooled_read")
        inv_ready = sem("inv_ready")
        pooled_ready = sem("pooled_ready")
        stats_ready = sem("stats_ready")
        mean_ready = sem("mean_ready")
        var_ready = sem("var_ready")
        std_ready = sem("std_ready")
        rstd_ready = sem("rstd_ready")
        normed_ready = sem("normed_ready")
        scaled_ready = sem("scaled_ready")
        result_ready = sem("result_ready")
        out_written = sem("out_written")

        def row_vector(v):
            return v.rearrange("(o d) -> o d", o=1)

        block = ctx.enter_context(nc.Block())

        @block.sync
        def _(sp):
            def load(g, s):
                sp.dma_start(xs[s][:, :, :].rearrange("p j d -> p (j d)"),
                             x_tiles[g * SLOTS + s]).then_inc(x_landed[s], 16)

            for s in range(SLOTS):
                load(0, s)
            with sp.Fori(1, ROUNDS) as g:
                for s in range(SLOTS):
                    sp.wait_ge(tiles_summed, (g - 1) * SLOTS + s + 1)
                    load(g, s)
            for g in range(ROUNDS):
                sp.wait_ge(result_ready, g + 1)
                sp.dma_start(out_rounds[g], result[:, g, :]).then_inc(out_written, 16)
            sp.wait_ge(out_written, 16 * ROUNDS)

        @block.gpsimd
        def _(pool):
            pool.memset(ident[:, :], 1.0).then_inc(sel_step, 1)
            pool.memset(sel[:, :], 1.0).then_inc(sel_step, 1)
            pool.wait_ge(sel_step, 2)
            pool.affine_select(out=ident[:, :], in_=ident[:, :], compare_op=ALU.is_equal, fill=0.0, base=0,
                               pattern=[[-1, P]], channel_multiplier=1).then_inc(consts_made, 1)
            pool.affine_select(out=sel[:, :], in_=sel[:, :], compare_op=ALU.is_ge, fill=0.0, base=SEGS * TB,
                               pattern=[[-SEGS, 3 * TB]], channel_multiplier=1).then_inc(sel_step, 1)
            pool.wait_ge(sel_step, 3)
            pool.affine_select(out=sel[:, :], in_=sel[:, :], compare_op=ALU.is_ge, fill=0.0,
                               base=SEGS - 1 - SEGS * TB,
                               pattern=[[SEGS, 3 * TB]], channel_multiplier=-1).then_inc(consts_made, 1)
            pool.iota(pos[:, :], pattern=[[1, ROWS]], base=0, channel_multiplier=ROWS,
                      allow_small_or_imprecise_dtypes=True).then_inc(consts_made, 1)
            pool.iota(len_off[:, :], pattern=[[L, TB]], base=0, channel_multiplier=0,
                      allow_small_or_imprecise_dtypes=True).then_inc(consts_made, 1)
            pool.memset(weights[:, :, :, :, :].rearrange("p a b j c -> p (a b j c)"), 0.0).then_inc(consts_made, 1)

            def multiply(g, i, k, first):
                s = 2 * i + k
                pool.wait_ge(x_landed[s], 16 * (g + 1))
                if s == 0 and first:
                    pool.wait_ge(consts_landed, 80)
                if s >= 2 or not first:
                    pool.wait_ge(act_scores, SLOTS * g + s - 1)
                pool.tensor_tensor(prods[:, k, :, :], xs[s][:, DVE_ROWS:ROWS, :],
                                   w_rep[:, :].unsqueeze(1).to_broadcast([P, POOL_ROWS, D]),
                                   ALU.mult).then_inc(prods_ready, 1)

            def spread(n, par, first):
                if first:
                    pool.wait_ge(consts_made, 5)
                pool.wait_ge(probs_ready, n + 1)
                for k in range(2):
                    pool.tensor_tensor(
                        weights[:, par, k, :, k * TB:(k + 1) * TB],
                        probs[:, par, k, :].unsqueeze(2).to_broadcast([P, ROWS, TB]),
                        sel[:, TB:2 * TB].unsqueeze(1).to_broadcast([P, ROWS, TB]),
                        ALU.mult).then_inc(weights_ready, 1)

            def round_(g, first):
                for i in range(GROUPS):
                    multiply(g, i, 0, first)
                    multiply(g, i, 1, first)
                    if i > 0 or not first:
                        n = GROUPS * g + i - 1
                        if i >= 3 or not first:
                            pool.wait_ge(tiles_summed, 2 * (n - 1))
                        spread(n, (i - 1) % 2, first)

            round_(0, True)
            with pool.Fori(1, ROUNDS) as g:
                round_(g, False)
            pool.wait_ge(tiles_summed, 2 * (GROUPS * ROUNDS - 2))
            spread(GROUPS * ROUNDS - 1, 1, False)

        @block.scalar
        def _(act):
            act.dma_start(w_rep[:, :], row_vector(w_att).broadcast_to([P, D])).then_inc(consts_landed, 16)
            act.dma_start(len_i[:, :], len_tiles).then_inc(consts_landed, 16)
            act.dma_start(b_rep[:, :], row_vector(b_att).broadcast_to([P, 1])).then_inc(consts_landed, 16)
            act.dma_start(gamma_rep[:, :], row_vector(ln_gamma).broadcast_to([P, D])).then_inc(consts_landed, 16)
            act.dma_start(beta_rep[:, :], row_vector(ln_beta).broadcast_to([P, D])).then_inc(consts_landed, 16)
            act.wait_ge(consts_landed, 80)
            act.copy(w_ps[:, 0:D], w_rep[:, :]).then_inc(w_ps_ready, 1)

            def sum_rows(g, i, k, first, lo, hi):
                s = 2 * i + k
                if lo == 0:
                    act.wait_ge(prods_ready, SLOTS * g + s + 1)
                    if k == 0 and (i >= 2 or not first):
                        act.wait_ge(masked_ready, GROUPS * g + i - 1)
                for r in range(lo, hi):
                    done = act.activation(prods[:, k, r, :], prods[:, k, r, :], ACT.Copy,
                                          accum_out=scores[:, i % 2, k, DVE_ROWS + r:DVE_ROWS + r + 1])
                    if r == POOL_ROWS - 1:
                        done.then_inc(act_scores, 1)

            def spread_max(n, par):
                act.wait_ge(batch_max_ready, n + 1)
                act.activation(neg_max_exp[:, par, :, :],
                               batch_max[:, par, :].unsqueeze(2).to_broadcast([2, TB, SEGS]),
                               ACT.Copy, scale=-1.0).then_inc(neg_max_spread, 1)

            def exponentials(n, par):
                act.wait_ge(neg_max_turned, n + 1)
                act.copy(neg_max[:, par, :], neg_max_ps[:, 0:2]).then_inc(neg_max_ready, 1)
                act.wait_ge(neg_max_ready, n + 1)
                for k in range(2):
                    done = act.activation(probs[:, par, k, :], masked[:, par, k, :], ACT.Exp,
                                          bias=neg_max[:, par, k:k + 1], accum_out=seg_sum[:, par, k:k + 1])
                done.then_inc(probs_ready, 1)

            def copy_partial(n, par):
                act.wait_ge(tiles_summed, 2 * n + 2)
                act.copy(partial[:, par, :], partial_ps[par][:, 0:D]).then_inc(partial_copied, 1)

            half = POOL_ROWS // 2

            def round_(g, first):
                for i in range(GROUPS):
                    n = GROUPS * g + i
                    before = i > 0 or not first
                    if i >= 2 or not first:
                        copy_partial(n - 2, i % 2)
                    sum_rows(g, i, 0, first, 0, POOL_ROWS)
                    sum_rows(g, i, 1, first, 0, half)
                    if before:
                        spread_max(n - 1, (i - 1) % 2)
                    sum_rows(g, i, 1, first, half, POOL_ROWS)
                    if before:
                        exponentials(n - 1, (i - 1) % 2)

            round_(0, True)
            with act.Fori(1, ROUNDS) as g:
                round_(g, False)
            last = GROUPS * ROUNDS - 1
            copy_partial(last - 1, 0)
            spread_max(last, 1)
            exponentials(last, 1)
            for g in range(ROUNDS):
                if g == ROUNDS - 1:
                    copy_partial(last, 1)
                act.wait_ge(var_ready, g + 1)
                act.activation(std[:, g:g + 1], var_eps[:, g:g + 1], ACT.Sqrt).then_inc(std_ready, 1)

        @block.tensor
        def _(pe):
            pe.wait_ge(consts_made, 5)
            pe.wait_ge(len_exp_ready, 1)
            pe.matmul(len_ps[:, 0:TILES], len_exp[:, :, :].rearrange("t b s -> t (b s)"),
                      ident[0:TILES, 0:TILES], start=True, stop=True).then_inc(len_p_ready, 1)

            def pair(g, i, first):
                n = GROUPS * g + i
                par = i % 2
                pe.wait_ge(seg_max_ready, n + 1)
                pe.matmul(seg_max_ps[0:2, 0:P], seg_max[:, par, :], ident[:, :],
                          start=True, stop=True).then_inc(seg_max_turned, 1)
                pe.wait_ge(neg_max_spread, n + 1)
                pe.matmul(neg_max_ps[:, 0:2], neg_max_exp[:, par, :, :].rearrange("t b s -> t (b s)"),
                          ident[0:2, 0:2], start=True, stop=True).then_inc(neg_max_turned, 1)
                for m in range(2 * ROWS):
                    k, j = divmod(m, ROWS)
                    q = m % GROUPS
                    if j == 0:
                        pe.wait_ge(weights_ready, SLOTS * g + 2 * i + k + 1)
                    done = pe.matmul(partial_ps[par][PB * q:PB * (q + 1), 0:D], weights[:, par, k, j, :],
                                     xs[2 * i + k][:, j, :], start=(m < GROUPS), stop=(m >= 2 * ROWS - GROUPS))
                    if j == ROWS - 1:
                        done.then_inc(tiles_summed, 1)
                if i == 0 and not first:
                    pe.wait_ge(pooled_read, g)
                pe.wait_ge(partial_copied, n + 1)
                rows = slice(PB * i, PB * (i + 1))
                pe.matmul(pooled_ps[rows, 0:D], fold[:, :], partial[:, par, :], start=True, stop=True)
                pe.matmul(pooled_ps[rows, D:D + 1], sel[:, TB:3 * TB], seg_sum[:, par, 0:1],
                          start=True, stop=False)
                pe.matmul(pooled_ps[rows, D:D + 1], sel[:, 0:2 * TB], seg_sum[:, par, 1:2],
                          start=False, stop=True).then_inc(pooled_summed, 1)

            for i in range(GROUPS):
                pair(0, i, True)
            with pe.Fori(1, ROUNDS) as g:
                for i in range(GROUPS):
                    pair(g, i, False)

        @block.vector
        def _(dve):
            dve.wait_ge(consts_landed, 80)
            dve.wait_ge(consts_made, 5)
            dve.tensor_copy(len_f[:, :], len_i[:, :]).then_inc(setup_dve, 1)
            dve.tensor_reduce(fold[:, :], ident[:, :].rearrange("p (q c) -> p c q", q=GROUPS), AX_X,
                              ALU.add).then_inc(setup_dve, 1)
            dve.wait_ge(setup_dve, 2)
            dve.tensor_tensor(len_end[:, :], len_f[:, :], len_off[:, :], ALU.add).then_inc(setup_dve, 1)
            dve.wait_ge(setup_dve, 3)
            dve.tensor_copy(len_exp[:, :, :],
                            len_end[:, :].unsqueeze(2).to_broadcast([TILES, TB, SEGS])).then_inc(len_exp_ready, 1)
            dve.wait_ge(len_p_ready, 1)
            dve.tensor_copy(len_p[:, :], len_ps[:, 0:TILES]).then_inc(setup_dve, 1)
            dve.wait_ge(setup_dve, 4)
            dve.tensor_tensor(is_pad[:, :, :], pos[:, :].unsqueeze(1).to_broadcast([P, TILES, ROWS]),
                              len_p[:, :].unsqueeze(2).to_broadcast([P, TILES, ROWS]),
                              ALU.is_ge).then_inc(setup_dve, 1)
            dve.wait_ge(setup_dve, 5)
            dve.tensor_scalar(penalty[:, :, :], is_pad[:, :, :], MASKED, b_rep[:, 0:1],
                              ALU.mult, ALU.add).then_inc(setup_dve, 1)
            dve.wait_ge(setup_dve, 6)
            dve.wait_ge(w_ps_ready, 1)

            def score_rows(g, i, k, lo, hi, first):
                if lo == 0:
                    dve.wait_ge(x_landed[2 * i + k], 16 * (g + 1))
                    if i > 0 or not first:
                        dve.wait_ge(dve_scores, SLOTS * g + 2 * i + k - 1)
                for j in range(lo, hi):
                    done = dve.tensor_tensor_reduce(dve_prods[:, k, j, :], xs[2 * i + k][:, j, :], w_ps[:, 0:D],
                                                    1.0, 0.0, ALU.mult, ALU.add,
                                                    scores[:, i % 2, k, j:j + 1])
                    if j == DVE_ROWS - 1:
                        done.then_inc(dve_scores, 1)

            def mask(g, i, n, par):
                dve.wait_ge(dve_scores, 2 * n + 2)
                dve.wait_ge(act_scores, 2 * n + 2)
                t = SLOTS * g + 2 * i
                dve.tensor_tensor(masked[:, par, :, :], scores[:, par, :, :], penalty[:, bass.ds(t, 2), :],
                                  ALU.add).then_inc(masked_ready, 1)

            def segment_max(n, par):
                dve.wait_ge(masked_ready, n + 1)
                dve.tensor_reduce(seg_max[:, par, :], masked[:, par, :, :], AX_X, ALU.max).then_inc(seg_max_ready, 1)

            def across_segments(n, par):
                dve.wait_ge(seg_max_turned, n + 1)
                dve.tensor_reduce(batch_max[:, par, :],
                                  seg_max_ps[0:2, 0:P].rearrange("t (b s) -> t b s", s=SEGS),
                                  AX_X, ALU.max).then_inc(batch_max_ready, 1)

            def invert_sums(g):
                dve.wait_ge(pooled_summed, GROUPS * (g + 1))
                dve.reciprocal(inv_sum[:, :], pooled_ps[:, D:D + 1]).then_inc(inv_ready, 1)

            def divide(g):
                dve.wait_ge(inv_ready, g + 1)
                dve.tensor_scalar(pooled[:, bass.ds(g, 1), :].rearrange("p o d -> p (o d)"),
                                  pooled_ps[:, 0:D], inv_sum[:, 0:1], None,
                                  ALU.mult).then_inc(pooled_read, 1)

            def moments(g):
                dve.wait_ge(pooled_read, g + 1)
                dve.bn_stats(stats[:, bass.ds(g, 1), :].rearrange("p o d -> p (o d)"),
                             pooled[:, bass.ds(g, 1), :].rearrange("p o d -> p (o d)")).then_inc(stats_ready, 1)

            def round_(g, first):
                for i in range(GROUPS):
                    before = i > 0 or not first
                    n = GROUPS * g + i - 1
                    par = (i - 1) % 2
                    score_rows(g, i, 0, 0, 8, first)
                    if before:
                        if i > 0:
                            mask(g, i - 1, n, par)
                        else:
                            mask(g - 1, GROUPS - 1, n, par)
                    score_rows(g, i, 0, 8, 10, first)
                    if before:
                        segment_max(n, par)
                    score_rows(g, i, 0, 10, DVE_ROWS, first)
                    if before:
                        across_segments(n, par)
                    score_rows(g, i, 1, 0, DVE_ROWS, first)
                    if i == 1 and not first:
                        invert_sums(g - 1)
                    if i == 1 and not first:
                        divide(g - 1)
                        moments(g - 1)

            round_(0, True)
            with dve.Fori(1, ROUNDS) as g:
                round_(g, False)
            last = GROUPS * ROUNDS - 1
            mask(ROUNDS - 1, GROUPS - 1, last, 1)
            segment_max(last, 1)
            across_segments(last, 1)

            def variance(g):
                dve.wait_ge(stats_ready, g + 1)
                dve.bn_aggr(mean_var[:, g, :], stats[:, g, :]).then_inc(mean_ready, 1)
                dve.wait_ge(mean_ready, g + 1)
                dve.tensor_scalar(var_eps[:, g:g + 1], mean_var[:, g, 1:2], LN_EPS, None,
                                  ALU.add).then_inc(var_ready, 1)

            def normalise(g):
                dve.wait_ge(std_ready, g + 1)
                dve.reciprocal(rstd[:, g:g + 1], std[:, g:g + 1]).then_inc(rstd_ready, 1)
                dve.wait_ge(rstd_ready, g + 1)
                dve.tensor_scalar(normed[:, g, :], pooled[:, g, :], mean_var[:, g, 0:1], rstd[:, g:g + 1],
                                  ALU.subtract, ALU.mult).then_inc(normed_ready, 1)
                dve.wait_ge(normed_ready, g + 1)
                dve.tensor_tensor(scaled[:, g, :], normed[:, g, :], gamma_rep[:, :], ALU.mult).then_inc(scaled_ready, 1)
                dve.wait_ge(scaled_ready, g + 1)
                dve.tensor_tensor(result[:, g, :], scaled[:, g, :], beta_rep[:, :], ALU.add).then_inc(result_ready, 1)

            for g in range(ROUNDS - 1):
                variance(g)
            for g in range(ROUNDS - 1):
                normalise(g)
            g = ROUNDS - 1
            invert_sums(g)
            divide(g)
            moments(g)
            variance(g)
            normalise(g)


_INS = ['r_padded_embeddings', 'r_lengths', 'L0_rec_w_att', 'L0_rec_b_att', 'L0_rec_ln_gamma', 'L0_rec_ln_beta']


def kernel(**inputs):
    import numpy as _np
    import concourse.bacc as _bacc
    from concourse import mybir as _mybir
    from concourse.bass_utils import run_bass_kernel_spmd as _run

    nc = _bacc.Bacc("TRN2", target_bir_lowering=False, num_devices=1)
    arrays, args = {}, []
    for name in _INS:
        a = _np.ascontiguousarray(inputs[name])
        arrays[f"in_{name}_dram"] = a
        args.append(nc.dram_tensor(f"in_{name}_dram", a.shape, _mybir.dt.from_np(a.dtype), kind="ExternalInput").ap())
    B, _, D = inputs['r_padded_embeddings'].shape
    args.append(nc.dram_tensor("out_dram", (B, D), _mybir.dt.float32, kind="ExternalOutput").ap())
    attention_pool_layernorm(nc, *args)
    r = _run(nc, [arrays], core_ids=[0])
    return r.results[0]["out_dram"]
```

```python
from contextlib import ExitStack

import concourse.bass as bass
from concourse import mybir

ALU = mybir.AluOpType
ACT = mybir.ActivationFunctionType
AX_X = mybir.AxisListType.X
F32 = mybir.dt.float32
I32 = mybir.dt.int32

P = 128
LN_EPS = 1e-5
MASKED = -3.0e38


def attention_pool_layernorm(nc, x, lengths, w_att, b_att, ln_gamma, ln_beta, out):
    B, L, D = x.shape
    SEGS = 8
    ROWS = L // SEGS
    TB = P // SEGS
    TILES = B // TB
    PB = 2 * TB
    GROUPS = P // PB
    SLOTS = 2 * GROUPS
    ROUNDS = TILES // SLOTS
    DVE_ROWS = 17
    POOL_ROWS = ROWS - DVE_ROWS
    MASK_AT = 6
    assert L % SEGS == 0 and D == P and PB == 32 and TILES % SLOTS == 0

    x_tiles = x.rearrange("(t b) (s j) d -> t (b s) (j d)", b=TB, s=SEGS)
    out_rounds = out.rearrange("(g p) d -> g p d", p=P)
    len_tiles = lengths.rearrange("(t b) -> t b", b=TB)

    with ExitStack() as ctx:
        def sb(name, shape, dt=F32):
            return ctx.enter_context(nc.sbuf_tensor(name, shape, dt))

        def psum(name, shape):
            return ctx.enter_context(nc.psum_tensor(name, shape, F32))

        def sem(name):
            return ctx.enter_context(nc.semaphore(name))

        xs = [sb(f"x_slot{s}", [P, ROWS, D]) for s in range(SLOTS)]
        w_rep = sb("w_rep", [P, D])
        gamma_rep = sb("gamma_rep", [P, D])
        beta_rep = sb("beta_rep", [P, D])
        b_rep = sb("b_rep", [P, 1])
        ident = sb("ident", [P, P])
        sel = sb("sel", [P, 3 * TB])
        fold = sb("fold", [P, PB])
        len_i = sb("len_i", [TILES, TB], I32)
        len_f = sb("len_f", [TILES, TB])
        len_off = sb("len_off", [TILES, TB])
        len_end = sb("len_end", [TILES, TB])
        len_exp = sb("len_exp", [TILES, TB, SEGS])
        len_p = sb("len_p", [P, TILES])
        pos = sb("pos", [P, ROWS])
        is_pad = sb("is_pad", [P, TILES, ROWS])
        penalty = sb("penalty", [P, TILES, ROWS])
        dve_prods = sb("dve_prods", [P, 2, DVE_ROWS, D])
        prods = sb("prods", [P, 2, POOL_ROWS, D])
        scores = sb("scores", [P, 2, 2, ROWS])
        masked = sb("masked", [P, 2, 2, ROWS])
        seg_max = sb("seg_max", [P, 2, 2])
        batch_max = sb("batch_max", [2, 2, TB])
        neg_max_exp = sb("neg_max_exp", [2, 2, TB, SEGS])
        neg_max = sb("neg_max", [P, 2, 2])
        probs = sb("probs", [P, 2, 2, ROWS])
        seg_sum = sb("seg_sum", [P, 2, 2])
        weights = sb("weights", [P, 2, 2, ROWS, PB])
        partial = sb("partial", [P, 2, D])
        inv_sum = sb("inv_sum", [P, 1])
        pooled = sb("pooled", [P, ROUNDS, D])
        stats = sb("stats", [P, ROUNDS, 6])
        mean_var = sb("mean_var", [P, ROUNDS, 2])
        var_eps = sb("var_eps", [P, ROUNDS])
        std = sb("std", [P, ROUNDS])
        rstd = sb("rstd", [P, ROUNDS])
        normed = sb("normed", [P, ROUNDS, D])
        scaled = sb("scaled", [P, ROUNDS, D])
        result = sb("result", [P, ROUNDS, D])

        w_ps = psum("w_ps", [P, 512])
        len_ps = psum("len_ps", [P, 512])
        seg_max_ps = psum("seg_max_ps", [P, 512])
        neg_max_ps = psum("neg_max_ps", [P, 512])
        partial_ps = [psum(f"partial_ps{k}", [P, 512]) for k in range(2)]
        pooled_ps = psum("pooled_ps", [P, 512])

        w_landed = sem("w_landed")
        len_landed = sem("len_landed")
        b_landed = sem("b_landed")
        gamma_landed = sem("gamma_landed")
        beta_landed = sem("beta_landed")
        x_landed = [sem(f"x_landed{s}") for s in range(SLOTS)]
        tiles_summed = sem("tiles_summed")
        sel_step = sem("sel_step")
        consts_made = sem("consts_made")
        setup_dve = sem("setup_dve")
        len_exp_ready = sem("len_exp_ready")
        len_p_ready = sem("len_p_ready")
        w_ps_ready = sem("w_ps_ready")
        prods_ready = sem("prods_ready")
        dve_scores = sem("dve_scores")
        act_scores = sem("act_scores")
        masked_ready = sem("masked_ready")
        seg_max_ready = sem("seg_max_ready")
        seg_max_turned = sem("seg_max_turned")
        batch_max_ready = sem("batch_max_ready")
        neg_max_spread = sem("neg_max_spread")
        neg_max_turned = sem("neg_max_turned")
        neg_max_ready = sem("neg_max_ready")
        probs_ready = sem("probs_ready")
        weights_ready = sem("weights_ready")
        partial_copied = sem("partial_copied")
        pooled_summed = sem("pooled_summed")
        pooled_read = sem("pooled_read")
        inv_ready = sem("inv_ready")
        pooled_ready = sem("pooled_ready")
        stats_ready = sem("stats_ready")
        mean_ready = sem("mean_ready")
        var_ready = sem("var_ready")
        std_ready = sem("std_ready")
        rstd_ready = sem("rstd_ready")
        normed_ready = sem("normed_ready")
        scaled_ready = sem("scaled_ready")
        result_ready = sem("result_ready")
        out_written = sem("out_written")

        def row_vector(v):
            return v.rearrange("(o d) -> o d", o=1)

        block = ctx.enter_context(nc.Block())

        @block.sync
        def _(sp):
            def load(g, s):
                sp.dma_start(xs[s][:, :, :].rearrange("p j d -> p (j d)"),
                             x_tiles[g * SLOTS + s]).then_inc(x_landed[s], 16)

            sp.dma_start(w_rep[:, :], row_vector(w_att).broadcast_to([P, D])).then_inc(w_landed, 16)
            sp.dma_start(len_i[:, :], len_tiles).then_inc(len_landed, 16)
            sp.dma_start(b_rep[:, :], row_vector(b_att).broadcast_to([P, 1])).then_inc(b_landed, 16)
            for s in range(SLOTS):
                load(0, s)
            sp.dma_start(gamma_rep[:, :], row_vector(ln_gamma).broadcast_to([P, D])).then_inc(gamma_landed, 16)
            sp.dma_start(beta_rep[:, :], row_vector(ln_beta).broadcast_to([P, D])).then_inc(beta_landed, 16)
            with sp.Fori(1, ROUNDS) as g:
                for s in range(SLOTS):
                    sp.wait_ge(tiles_summed, (g - 1) * SLOTS + s + 1)
                    load(g, s)
            for g in range(ROUNDS):
                sp.wait_ge(result_ready, g + 1)
                sp.dma_start(out_rounds[g], result[:, g, :]).then_inc(out_written, 16)
            sp.wait_ge(out_written, 16 * ROUNDS)

        @block.gpsimd
        def _(pool):
            pool.memset(ident[:, :], 1.0).then_inc(sel_step, 1)
            pool.memset(sel[:, :], 1.0).then_inc(sel_step, 1)
            pool.wait_ge(sel_step, 2)
            pool.affine_select(out=ident[:, :], in_=ident[:, :], compare_op=ALU.is_equal, fill=0.0, base=0,
                               pattern=[[-1, P]], channel_multiplier=1).then_inc(consts_made, 1)
            pool.affine_select(out=sel[:, :], in_=sel[:, :], compare_op=ALU.is_ge, fill=0.0, base=SEGS * TB,
                               pattern=[[-SEGS, 3 * TB]], channel_multiplier=1).then_inc(sel_step, 1)
            pool.wait_ge(sel_step, 3)
            pool.affine_select(out=sel[:, :], in_=sel[:, :], compare_op=ALU.is_ge, fill=0.0,
                               base=SEGS - 1 - SEGS * TB,
                               pattern=[[SEGS, 3 * TB]], channel_multiplier=-1).then_inc(consts_made, 1)
            pool.iota(pos[:, :], pattern=[[1, ROWS]], base=0, channel_multiplier=ROWS,
                      allow_small_or_imprecise_dtypes=True).then_inc(consts_made, 1)
            pool.iota(len_off[:, :], pattern=[[L, TB]], base=0, channel_multiplier=0,
                      allow_small_or_imprecise_dtypes=True).then_inc(consts_made, 1)
            pool.memset(weights[:, :, :, :, :].rearrange("p a b j c -> p (a b j c)"), 0.0).then_inc(consts_made, 1)

            def multiply(g, i, k, first):
                s = 2 * i + k
                pool.wait_ge(x_landed[s], 16 * (g + 1))
                if s == 0 and first:
                    pool.wait_ge(w_landed, 16)
                if s >= 2 or not first:
                    pool.wait_ge(act_scores, SLOTS * g + s - 1)
                pool.tensor_tensor(prods[:, k, :, :], xs[s][:, DVE_ROWS:ROWS, :],
                                   w_rep[:, :].unsqueeze(1).to_broadcast([P, POOL_ROWS, D]),
                                   ALU.mult).then_inc(prods_ready, 1)

            def spread(n, par, first):
                if first:
                    pool.wait_ge(consts_made, 5)
                pool.wait_ge(probs_ready, n + 1)
                for k in range(2):
                    pool.tensor_tensor(
                        weights[:, par, k, :, k * TB:(k + 1) * TB],
                        probs[:, par, k, :].unsqueeze(2).to_broadcast([P, ROWS, TB]),
                        sel[:, TB:2 * TB].unsqueeze(1).to_broadcast([P, ROWS, TB]),
                        ALU.mult).then_inc(weights_ready, 1)

            def round_(g, first):
                for i in range(GROUPS):
                    multiply(g, i, 0, first)
                    multiply(g, i, 1, first)
                    if i > 0 or not first:
                        n = GROUPS * g + i - 1
                        if i >= 3 or not first:
                            pool.wait_ge(tiles_summed, 2 * (n - 1))
                        spread(n, (i - 1) % 2, first)

            round_(0, True)
            with pool.Fori(1, ROUNDS) as g:
                round_(g, False)
            pool.wait_ge(tiles_summed, 2 * (GROUPS * ROUNDS - 2))
            spread(GROUPS * ROUNDS - 1, 1, False)

        @block.scalar
        def _(act):
            act.wait_ge(w_landed, 16)
            act.copy(w_ps[:, 0:D], w_rep[:, :]).then_inc(w_ps_ready, 1)

            def sum_rows(g, i, k, first, lo, hi):
                s = 2 * i + k
                if lo == 0:
                    act.wait_ge(prods_ready, SLOTS * g + s + 1)
                    if k == 0 and (i >= 2 or not first):
                        act.wait_ge(masked_ready, GROUPS * g + i - 1)
                for r in range(lo, hi):
                    done = act.activation(prods[:, k, r, :], prods[:, k, r, :], ACT.Copy,
                                          accum_out=scores[:, i % 2, k, DVE_ROWS + r:DVE_ROWS + r + 1])
                    if r == POOL_ROWS - 1:
                        done.then_inc(act_scores, 1)

            def spread_max(n, par):
                act.wait_ge(batch_max_ready, n + 1)
                act.activation(neg_max_exp[:, par, :, :],
                               batch_max[:, par, :].unsqueeze(2).to_broadcast([2, TB, SEGS]),
                               ACT.Copy, scale=-1.0).then_inc(neg_max_spread, 1)

            def exponentials(n, par):
                act.wait_ge(neg_max_turned, n + 1)
                act.copy(neg_max[:, par, :], neg_max_ps[:, 0:2]).then_inc(neg_max_ready, 1)
                act.wait_ge(neg_max_ready, n + 1)
                for k in range(2):
                    done = act.activation(probs[:, par, k, :], masked[:, par, k, :], ACT.Exp,
                                          bias=neg_max[:, par, k:k + 1], accum_out=seg_sum[:, par, k:k + 1])
                done.then_inc(probs_ready, 1)

            def copy_partial(n, par):
                act.wait_ge(tiles_summed, 2 * n + 2)
                act.copy(partial[:, par, :], partial_ps[par][:, 0:D]).then_inc(partial_copied, 1)

            def round_(g, first):
                for i in range(GROUPS):
                    n = GROUPS * g + i
                    before = i > 0 or not first
                    if before:
                        spread_max(n - 1, (i - 1) % 2)
                    sum_rows(g, i, 0, first, 0, 2)
                    if before:
                        exponentials(n - 1, (i - 1) % 2)
                    sum_rows(g, i, 0, first, 2, POOL_ROWS)
                    if i >= 2 or not first:
                        copy_partial(n - 2, i % 2)
                    sum_rows(g, i, 1, first, 0, POOL_ROWS)

            round_(0, True)
            with act.Fori(1, ROUNDS) as g:
                round_(g, False)
            last = GROUPS * ROUNDS - 1
            spread_max(last, 1)
            exponentials(last, 1)
            copy_partial(last - 1, 0)
            for g in range(ROUNDS):
                if g == ROUNDS - 1:
                    copy_partial(last, 1)
                act.wait_ge(var_ready, g + 1)
                act.activation(std[:, g:g + 1], var_eps[:, g:g + 1], ACT.Sqrt).then_inc(std_ready, 1)

        @block.tensor
        def _(pe):
            pe.wait_ge(consts_made, 5)
            pe.wait_ge(len_exp_ready, 1)
            pe.matmul(len_ps[:, 0:TILES], len_exp[:, :, :].rearrange("t b s -> t (b s)"),
                      ident[0:TILES, 0:TILES], start=True, stop=True).then_inc(len_p_ready, 1)

            def turn_max(n, par):
                pe.wait_ge(seg_max_ready, n + 1)
                pe.matmul(seg_max_ps[0:2, 0:P], seg_max[:, par, :], ident[:, :],
                          start=True, stop=True).then_inc(seg_max_turned, 1)

            def turn_back(n, par):
                pe.wait_ge(neg_max_spread, n + 1)
                pe.matmul(neg_max_ps[:, 0:2], neg_max_exp[:, par, :, :].rearrange("t b s -> t (b s)"),
                          ident[0:2, 0:2], start=True, stop=True).then_inc(neg_max_turned, 1)

            def weighted_sums(n, i, k, lo, hi):
                if lo == 0:
                    pe.wait_ge(weights_ready, 2 * n + k + 1)
                for j in range(lo, hi):
                    m = k * ROWS + j
                    q = m % GROUPS
                    done = pe.matmul(partial_ps[i % 2][PB * q:PB * (q + 1), 0:D], weights[:, i % 2, k, j, :],
                                     xs[2 * i + k][:, j, :], start=(m < GROUPS), stop=(m >= 2 * ROWS - GROUPS))
                    if j == ROWS - 1:
                        done.then_inc(tiles_summed, 1)

            def fold_groups(n, i):
                pe.wait_ge(partial_copied, n + 1)
                rows = slice(PB * i, PB * (i + 1))
                par = i % 2
                pe.matmul(pooled_ps[rows, 0:D], fold[:, :], partial[:, par, :], start=True, stop=True)
                pe.matmul(pooled_ps[rows, D:D + 1], sel[:, TB:3 * TB], seg_sum[:, par, 0:1],
                          start=True, stop=False)
                pe.matmul(pooled_ps[rows, D:D + 1], sel[:, 0:2 * TB], seg_sum[:, par, 1:2],
                          start=False, stop=True).then_inc(pooled_summed, 1)

            half = ROWS // 2

            def round_(g, first):
                for i in range(GROUPS):
                    n = GROUPS * g + i
                    i1 = (i - 1) % GROUPS
                    i2 = (i - 2) % GROUPS
                    if i > 0 or not first:
                        turn_max(n - 1, i1 % 2)
                    if i >= 2 or not first:
                        weighted_sums(n - 2, i2, 1, 0, half)
                    if i > 0 or not first:
                        turn_back(n - 1, i1 % 2)
                    if i >= 2 or not first:
                        weighted_sums(n - 2, i2, 1, half, ROWS)
                    if i > 0 or not first:
                        weighted_sums(n - 1, i1, 0, 0, ROWS)
                    if i == 2 and not first:
                        pe.wait_ge(pooled_read, g)
                    if i >= 2 or not first:
                        fold_groups(n - 2, i2)

            round_(0, True)
            with pe.Fori(1, ROUNDS) as g:
                round_(g, False)
            last = GROUPS * ROUNDS - 1
            turn_max(last, 1)
            weighted_sums(last - 1, GROUPS - 2, 1, 0, half)
            turn_back(last, 1)
            weighted_sums(last - 1, GROUPS - 2, 1, half, ROWS)
            weighted_sums(last, GROUPS - 1, 0, 0, ROWS)
            fold_groups(last - 1, GROUPS - 2)
            weighted_sums(last, GROUPS - 1, 1, 0, ROWS)
            fold_groups(last, GROUPS - 1)

        @block.vector
        def _(dve):
            dve.wait_ge(len_landed, 16)
            dve.wait_ge(consts_made, 5)
            dve.tensor_copy(len_f[:, :], len_i[:, :]).then_inc(setup_dve, 1)
            dve.tensor_reduce(fold[:, :], ident[:, :].rearrange("p (q c) -> p c q", q=GROUPS), AX_X,
                              ALU.add).then_inc(setup_dve, 1)
            dve.wait_ge(setup_dve, 2)
            dve.tensor_tensor(len_end[:, :], len_f[:, :], len_off[:, :], ALU.add).then_inc(setup_dve, 1)
            dve.wait_ge(setup_dve, 3)
            dve.tensor_copy(len_exp[:, :, :],
                            len_end[:, :].unsqueeze(2).to_broadcast([TILES, TB, SEGS])).then_inc(len_exp_ready, 1)
            dve.wait_ge(len_p_ready, 1)
            dve.tensor_copy(len_p[:, :], len_ps[:, 0:TILES]).then_inc(setup_dve, 1)
            dve.wait_ge(setup_dve, 4)
            dve.tensor_tensor(is_pad[:, :, :], pos[:, :].unsqueeze(1).to_broadcast([P, TILES, ROWS]),
                              len_p[:, :].unsqueeze(2).to_broadcast([P, TILES, ROWS]),
                              ALU.is_ge).then_inc(setup_dve, 1)
            dve.wait_ge(setup_dve, 5)
            dve.wait_ge(b_landed, 16)
            dve.tensor_scalar(penalty[:, :, :], is_pad[:, :, :], MASKED, b_rep[:, 0:1],
                              ALU.mult, ALU.add).then_inc(setup_dve, 1)
            dve.wait_ge(setup_dve, 6)
            dve.wait_ge(w_ps_ready, 1)

            def score_rows(g, i, k, lo, hi, first):
                if lo == 0:
                    dve.wait_ge(x_landed[2 * i + k], 16 * (g + 1))
                    if i > 0 or not first:
                        dve.wait_ge(dve_scores, SLOTS * g + 2 * i + k - 1)
                for j in range(lo, hi):
                    done = dve.tensor_tensor_reduce(dve_prods[:, k, j, :], xs[2 * i + k][:, j, :], w_ps[:, 0:D],
                                                    1.0, 0.0, ALU.mult, ALU.add,
                                                    scores[:, i % 2, k, j:j + 1])
                    if j == DVE_ROWS - 1:
                        done.then_inc(dve_scores, 1)

            def mask(g, i, n, par):
                dve.wait_ge(dve_scores, 2 * n + 2)
                dve.wait_ge(act_scores, 2 * n + 2)
                t = SLOTS * g + 2 * i
                dve.tensor_tensor(masked[:, par, :, :], scores[:, par, :, :], penalty[:, bass.ds(t, 2), :],
                                  ALU.add).then_inc(masked_ready, 1)

            def segment_max(n, par):
                dve.wait_ge(masked_ready, n + 1)
                dve.tensor_reduce(seg_max[:, par, :], masked[:, par, :, :], AX_X, ALU.max).then_inc(seg_max_ready, 1)

            def across_segments(n, par):
                dve.wait_ge(seg_max_turned, n + 1)
                dve.tensor_reduce(batch_max[:, par, :],
                                  seg_max_ps[0:2, 0:P].rearrange("t (b s) -> t b s", s=SEGS),
                                  AX_X, ALU.max).then_inc(batch_max_ready, 1)

            def invert_sums(g):
                dve.wait_ge(pooled_summed, GROUPS * (g + 1))
                dve.reciprocal(inv_sum[:, :], pooled_ps[:, D:D + 1]).then_inc(inv_ready, 1)

            def divide(g):
                dve.wait_ge(inv_ready, g + 1)
                dve.tensor_scalar(pooled[:, bass.ds(g, 1), :].rearrange("p o d -> p (o d)"),
                                  pooled_ps[:, 0:D], inv_sum[:, 0:1], None,
                                  ALU.mult).then_inc(pooled_read, 1)

            def moments(g):
                dve.wait_ge(pooled_read, g + 1)
                dve.bn_stats(stats[:, bass.ds(g, 1), :].rearrange("p o d -> p (o d)"),
                             pooled[:, bass.ds(g, 1), :].rearrange("p o d -> p (o d)")).then_inc(stats_ready, 1)

            def round_(g, first):
                for i in range(GROUPS):
                    before = i > 0 or not first
                    n = GROUPS * g + i - 1
                    par = (i - 1) % 2
                    score_rows(g, i, 0, 0, MASK_AT, first)
                    if before:
                        if i > 0:
                            mask(g, i - 1, n, par)
                        else:
                            mask(g - 1, GROUPS - 1, n, par)
                    score_rows(g, i, 0, MASK_AT, MASK_AT + 2, first)
                    if before:
                        segment_max(n, par)
                    score_rows(g, i, 0, MASK_AT + 2, MASK_AT + 6, first)
                    if before:
                        across_segments(n, par)
                    score_rows(g, i, 0, MASK_AT + 6, DVE_ROWS, first)
                    score_rows(g, i, 1, 0, 10, first)
                    if i == 2 and not first:
                        invert_sums(g - 1)
                    score_rows(g, i, 1, 10, DVE_ROWS, first)
                    if i == 2 and not first:
                        divide(g - 1)
                        moments(g - 1)

            round_(0, True)
            with dve.Fori(1, ROUNDS) as g:
                round_(g, False)
            last = GROUPS * ROUNDS - 1
            mask(ROUNDS - 1, GROUPS - 1, last, 1)
            segment_max(last, 1)
            across_segments(last, 1)

            def variance(g):
                dve.wait_ge(stats_ready, g + 1)
                dve.bn_aggr(mean_var[:, g, :], stats[:, g, :]).then_inc(mean_ready, 1)
                dve.wait_ge(mean_ready, g + 1)
                dve.tensor_scalar(var_eps[:, g:g + 1], mean_var[:, g, 1:2], LN_EPS, None,
                                  ALU.add).then_inc(var_ready, 1)

            def normalise(g):
                dve.wait_ge(std_ready, g + 1)
                dve.reciprocal(rstd[:, g:g + 1], std[:, g:g + 1]).then_inc(rstd_ready, 1)
                dve.wait_ge(rstd_ready, g + 1)
                dve.tensor_scalar(normed[:, g, :], pooled[:, g, :], mean_var[:, g, 0:1], rstd[:, g:g + 1],
                                  ALU.subtract, ALU.mult).then_inc(normed_ready, 1)
                dve.wait_ge(normed_ready, g + 1)
                dve.tensor_tensor(scaled[:, g, :], normed[:, g, :], gamma_rep[:, :], ALU.mult).then_inc(scaled_ready, 1)
                dve.wait_ge(scaled_ready, g + 1)
                dve.tensor_tensor(result[:, g, :], scaled[:, g, :], beta_rep[:, :], ALU.add).then_inc(result_ready, 1)

            for g in range(ROUNDS - 1):
                variance(g)
            dve.wait_ge(gamma_landed, 16)
            dve.wait_ge(beta_landed, 16)
            for g in range(ROUNDS - 1):
                normalise(g)
            g = ROUNDS - 1
            invert_sums(g)
            divide(g)
            moments(g)
            variance(g)
            normalise(g)


_INS = ['r_padded_embeddings', 'r_lengths', 'L0_rec_w_att', 'L0_rec_b_att', 'L0_rec_ln_gamma', 'L0_rec_ln_beta']


def kernel(**inputs):
    import numpy as _np
    import concourse.bacc as _bacc
    from concourse import mybir as _mybir
    from concourse.bass_utils import run_bass_kernel_spmd as _run

    nc = _bacc.Bacc("TRN2", target_bir_lowering=False, num_devices=1)
    arrays, args = {}, []
    for name in _INS:
        a = _np.ascontiguousarray(inputs[name])
        arrays[f"in_{name}_dram"] = a
        args.append(nc.dram_tensor(f"in_{name}_dram", a.shape, _mybir.dt.from_np(a.dtype), kind="ExternalInput").ap())
    B, _, D = inputs['r_padded_embeddings'].shape
    args.append(nc.dram_tensor("out_dram", (B, D), _mybir.dt.float32, kind="ExternalOutput").ap())
    attention_pool_layernorm(nc, *args)
    r = _run(nc, [arrays], core_ids=[0])
    return r.results[0]["out_dram"]
```

```python
from contextlib import ExitStack

import concourse.bass as bass
from concourse import mybir

ALU = mybir.AluOpType
ACT = mybir.ActivationFunctionType
AX_X = mybir.AxisListType.X
F32 = mybir.dt.float32
I32 = mybir.dt.int32

P = 128
LN_EPS = 1e-5
MASKED = -3.0e38


def attention_pool_layernorm(nc, x, lengths, w_att, b_att, ln_gamma, ln_beta, out):
    B, L, D = x.shape
    SEGS = 8
    ROWS = L // SEGS
    TB = P // SEGS
    TILES = B // TB
    PB = 2 * TB
    GROUPS = P // PB
    SLOTS = 2 * GROUPS
    ROUNDS = TILES // SLOTS
    BUFS = 4
    QUAD = 32
    LOADS = ((0, 8), (8, 17), (17, ROWS))
    POOL_PARTS = ((3, 8), (8, 12))
    POOL_FIRST, POOL_END = POOL_PARTS[0][0], POOL_PARTS[-1][1]
    POOL_ROWS = POOL_END - POOL_FIRST
    DVE_ROWS = [j for j in range(ROWS) if not POOL_FIRST <= j < POOL_END]
    EXP_AT = POOL_FIRST + 2
    DVE_SUMS = 12
    dve_load = {min(j for j in DVE_ROWS if lo <= j < hi): k for k, (lo, hi) in enumerate(LOADS)}
    pool_load = {part: k for part in POOL_PARTS for k, (lo, hi) in enumerate(LOADS) if lo <= part[0] and part[1] <= hi}
    assert all(part in pool_load for part in POOL_PARTS)
    assert L % SEGS == 0 and D == P and PB == 32 and TILES % SLOTS == 0 and SLOTS % BUFS == 0

    x_tiles = x.rearrange("(t b) (s j) d -> t (b s) (j d)", b=TB, s=SEGS)
    out_rounds = out.rearrange("(g p) d -> p g d", p=P)
    len_tiles = lengths.rearrange("(t b) -> t b", b=TB)

    with ExitStack() as ctx:
        def sb(name, shape, dt=F32):
            return ctx.enter_context(nc.sbuf_tensor(name, shape, dt))

        def psum(name, shape):
            return ctx.enter_context(nc.psum_tensor(name, shape, F32))

        def sem(name):
            return ctx.enter_context(nc.semaphore(name))

        xs = [sb(f"x_slot{s}", [P, ROWS, D]) for s in range(SLOTS)]
        w_rep = sb("w_rep", [P, D])
        gamma_rep = sb("gamma_rep", [P, D])
        beta_rep = sb("beta_rep", [P, D])
        b_rep = sb("b_rep", [P, 1])
        ident = sb("ident", [P, P])
        sel = sb("sel", [P, 3 * TB])
        fold = sb("fold", [P, PB])
        len_i = sb("len_i", [TILES, TB], I32)
        len_f = sb("len_f", [TILES, TB])
        len_off = sb("len_off", [TILES, TB])
        len_end = sb("len_end", [TILES, TB])
        len_exp = sb("len_exp", [TILES, TB, SEGS])
        len_p = sb("len_p", [P, TILES])
        pos = sb("pos", [P, ROWS])
        is_pad = sb("is_pad", [P, TILES, ROWS])
        penalty = sb("penalty", [P, TILES, ROWS])
        dve_prods = sb("dve_prods", [P, 2, ROWS - POOL_ROWS, D])
        pool_prods = sb("pool_prods", [P, 2, POOL_ROWS, D])
        scores = sb("scores", [P, BUFS, ROWS])
        masked = sb("masked", [P, BUFS, ROWS])
        seg_max = sb("seg_max", [P, BUFS, QUAD])
        turned = sb("turned", [P, BUFS, QUAD])
        batch_max = sb("batch_max", [P, BUFS, QUAD // SEGS])
        spread_max = sb("spread_max", [P, BUFS, QUAD])
        neg_max = sb("neg_max", [P, BUFS, QUAD])
        probs = sb("probs", [P, BUFS, ROWS])
        seg_sum = sb("seg_sum", [P, BUFS])
        weights = sb("weights", [P, BUFS, ROWS, PB])
        row_sums = sb("row_sums", [P, 2, D])
        partial = sb("partial", [P, 2, D])
        raw = sb("raw", [P, ROUNDS, D])
        stats = sb("stats", [P, 6])
        mean_var = sb("mean_var", [P, 2])
        var = sb("var", [P, ROUNDS])
        eps_z2 = sb("eps_z2", [P, ROUNDS])
        std = sb("std", [P, ROUNDS])
        rstd = sb("rstd", [P, ROUNDS])
        scaled = sb("scaled", [P, ROUNDS, D])
        result = sb("result", [P, ROUNDS, D])

        w_ps = psum("w_ps", [P, 512])
        len_ps = psum("len_ps", [P, 512])
        partial_ps = [psum(f"partial_ps{k}", [P, 512]) for k in range(2)]
        raw_ps = psum("raw_ps", [P, 512])
        z_ps = psum("z_ps", [P, 512])

        w_landed = sem("w_landed")
        len_landed = sem("len_landed")
        b_landed = sem("b_landed")
        gamma_landed = sem("gamma_landed")
        beta_landed = sem("beta_landed")
        select_step = sem("select_step")
        consts_made = sem("consts_made")
        zeros_written = sem("zeros_written")
        setup_step = sem("setup_step")
        len_exp_ready = sem("len_exp_ready")
        len_p_ready = sem("len_p_ready")
        w_ps_ready = sem("w_ps_ready")
        x_landed = [[sem(f"x_landed{s}_{lo}") for lo, _ in LOADS] for s in range(SLOTS)]
        dve_scores = sem("dve_scores")
        prods_ready = sem("prods_ready")
        act_scores = sem("act_scores")
        masked_ready = sem("masked_ready")
        seg_max_ready = sem("seg_max_ready")
        turned_ready = sem("turned_ready")
        batch_max_ready = sem("batch_max_ready")
        spread_max_ready = sem("spread_max_ready")
        neg_max_ready = sem("neg_max_ready")
        probs_ready = sem("probs_ready")
        weights_ready = sem("weights_ready")
        row_added = sem("row_added")
        tiles_summed = sem("tiles_summed")
        partial_copied = sem("partial_copied")
        raw_summed = sem("raw_summed")
        z_summed = sem("z_summed")
        raw_copied = sem("raw_copied")
        stats_ready = sem("stats_ready")
        mean_var_ready = sem("mean_var_ready")
        eps_z2_ready = sem("eps_z2_ready")
        std_ready = sem("std_ready")
        rstd_ready = sem("rstd_ready")
        var_ready = sem("var_ready")
        scaled_ready = sem("scaled_ready")
        result_ready = sem("result_ready")
        out_written = sem("out_written")

        def halves(rows):
            return ((0, (rows + 1) // 2), ((rows + 1) // 2, rows))

        def row_vector(v):
            return v.rearrange("(o d) -> o d", o=1)

        def each_step(step, eng):
            for s in range(SLOTS):
                step(0, s, lambda back, s=s: (s - back, s - back) if s >= back else None)
            with eng.Fori(1, ROUNDS) as g:
                for s in range(SLOTS):
                    step(g, s, lambda back, g=g, s=s: (SLOTS * g + s - back, (s - back) % SLOTS))

        LAST, LAST_ROUND = TILES - 1, ROUNDS - 1

        block = ctx.enter_context(nc.Block())

        @block.sync
        def _(sp):
            def load(g, s, loads=slice(0, None)):
                for (lo, hi), landed in list(zip(LOADS, x_landed[s]))[loads]:
                    sp.dma_start(xs[s][:, lo:hi, :].rearrange("p j d -> p (j d)"),
                                 x_tiles[g * SLOTS + s, :, lo * D:hi * D]).then_inc(landed, 16)

            load(0, 0, slice(0, 1))
            sp.dma_start(w_rep[:, :], row_vector(w_att).broadcast_to([P, D])).then_inc(w_landed, 16)
            sp.dma_start(len_i[:, :], len_tiles).then_inc(len_landed, 16)
            sp.dma_start(b_rep[:, :], row_vector(b_att).broadcast_to([P, 1])).then_inc(b_landed, 16)
            load(0, 0, slice(1, None))
            for s in range(1, SLOTS):
                load(0, s)
            sp.dma_start(gamma_rep[:, :], row_vector(ln_gamma).broadcast_to([P, D])).then_inc(gamma_landed, 16)
            sp.dma_start(beta_rep[:, :], row_vector(ln_beta).broadcast_to([P, D])).then_inc(beta_landed, 16)
            with sp.Fori(1, ROUNDS) as g:
                for s in range(SLOTS):
                    sp.wait_ge(tiles_summed, (g - 1) * SLOTS + s + 1)
                    load(g, s)
            sp.wait_ge(result_ready, LAST_ROUND)
            sp.dma_start(out_rounds[:, 0:LAST_ROUND, :], result[:, 0:LAST_ROUND, :]).then_inc(out_written, 16)
            sp.wait_ge(result_ready, ROUNDS)
            sp.dma_start(out_rounds[:, LAST_ROUND, :], result[:, LAST_ROUND, :]).then_inc(out_written, 16)
            sp.wait_ge(out_written, 2 * 16)

        @block.gpsimd
        def _(pool):
            pool.memset(ident[:, :], 1.0).then_inc(select_step, 1)
            pool.memset(sel[:, :], 1.0).then_inc(select_step, 1)
            pool.wait_ge(select_step, 2)
            pool.affine_select(out=ident[:, :], in_=ident[:, :], compare_op=ALU.is_equal, fill=0.0, base=0,
                               pattern=[[-1, P]], channel_multiplier=1).then_inc(consts_made, 1)
            pool.affine_select(out=sel[:, :], in_=sel[:, :], compare_op=ALU.is_ge, fill=0.0, base=SEGS * TB,
                               pattern=[[-SEGS, 3 * TB]], channel_multiplier=1).then_inc(select_step, 1)
            pool.wait_ge(select_step, 3)
            pool.affine_select(out=sel[:, :], in_=sel[:, :], compare_op=ALU.is_ge, fill=0.0,
                               base=SEGS - 1 - SEGS * TB,
                               pattern=[[SEGS, 3 * TB]], channel_multiplier=-1).then_inc(consts_made, 1)
            pool.iota(pos[:, :], pattern=[[1, ROWS]], base=0, channel_multiplier=ROWS,
                      allow_small_or_imprecise_dtypes=True).then_inc(consts_made, 1)
            pool.iota(len_off[:, :], pattern=[[L, TB]], base=0, channel_multiplier=0,
                      allow_small_or_imprecise_dtypes=True).then_inc(consts_made, 1)
            pool.memset(seg_max[:, :, :], 0.0).then_inc(zeros_written, 1)
            pool.memset(weights[:, :, :, :].rearrange("p b j c -> p (b j c)"), 0.0).then_inc(zeros_written, 1)
            pool.wait_ge(consts_made, 4)
            pool.wait_ge(zeros_written, 2)
            pool.wait_ge(w_landed, 16)

            def multiply(g, s, two_back):
                if two_back:
                    pool.wait_ge(act_scores, two_back[0] + 1)
                for lo, hi in POOL_PARTS:
                    pool.wait_ge(x_landed[s][pool_load[lo, hi]], 16 * (g + 1))
                    pool.tensor_tensor(pool_prods[:, s % 2, lo - POOL_FIRST:hi - POOL_FIRST, :], xs[s][:, lo:hi, :],
                                       w_rep[:, :].unsqueeze(1).to_broadcast([P, hi - lo, D]),
                                       ALU.mult).then_inc(prods_ready, 1)

            def spread(t, s, reused, rows=ROWS):
                b, half = s % BUFS, s % 2
                pool.wait_ge(probs_ready, t + 1)
                if reused:
                    pool.wait_ge(tiles_summed, t - BUFS + 1)
                for lo, hi in halves(rows):
                    pool.tensor_tensor(
                        weights[:, b, lo:hi, half * TB:(half + 1) * TB],
                        probs[:, b, lo:hi].unsqueeze(2).to_broadcast([P, hi - lo, TB]),
                        sel[:, TB:2 * TB].unsqueeze(1).to_broadcast([P, hi - lo, TB]),
                        ALU.mult).then_inc(weights_ready, 1)

            def step(g, s, back):
                multiply(g, s, back(2))
                if back(1):
                    spread(*back(1), reused=back(1 + BUFS) is not None)

            each_step(step, pool)
            spread(LAST, LAST % SLOTS, True, rows=ROWS - DVE_SUMS)

        @block.scalar
        def _(act):
            act.wait_ge(w_landed, 16)
            act.copy(w_ps[:, 0:D], w_rep[:, :]).then_inc(w_ps_ready, 1)

            def sum_row(s, j):
                prods = pool_prods[:, s % 2, j - POOL_FIRST, :]
                done = act.activation(prods, prods, ACT.Copy, accum_out=scores[:, s % BUFS, j:j + 1])
                if j == POOL_END - 1:
                    done.then_inc(act_scores, 1)

            def exponentials(t, s, z_pairs):
                b = s % BUFS
                if z_pairs is not None:
                    act.wait_ge(z_summed, z_pairs)
                act.wait_ge(neg_max_ready, t + 1)
                act.activation(probs[:, b, :], masked[:, b, :], ACT.Exp, bias=neg_max[:, b, 0:1],
                               accum_out=seg_sum[:, b:b + 1]).then_inc(probs_ready, 1)

            def copy_partial(t, s):
                par = (s // 2) % 2
                act.wait_ge(tiles_summed, t + 2)
                act.copy(partial[:, par, :], partial_ps[par][:, 0:D]).then_inc(partial_copied, 1)

            def step(g, s, back):
                t = SLOTS * g + s
                if back(BUFS):
                    act.wait_ge(masked_ready, back(BUFS)[0] + 1)
                for n, (lo, hi) in enumerate(POOL_PARTS):
                    act.wait_ge(prods_ready, len(POOL_PARTS) * t + n + 1)
                    for j in range(lo, hi):
                        if j == EXP_AT and back(1):
                            pairs = GROUPS * g + (s - 1 - BUFS) // 2 + 1 if back(1 + BUFS) else None
                            exponentials(*back(1), pairs)
                        sum_row(s, j)
                if s % 2 == 1 and back(3):
                    copy_partial(*back(3))
                if s == 1 and back(SLOTS):
                    square_z(g - 1)

            def square_z(g):
                act.wait_ge(z_summed, GROUPS * (g + 1))
                act.activation(eps_z2[:, bass.ds(g, 1)], z_ps[:, 0:1], ACT.Square,
                               scale=LN_EPS ** 0.5).then_inc(eps_z2_ready, 1)

            each_step(step, act)
            exponentials(LAST, LAST % SLOTS, (LAST - BUFS) // 2 + 1)

            def deviation(g):
                act.wait_ge(eps_z2_ready, g + 1)
                if g == LAST_ROUND:
                    act.wait_ge(mean_var_ready, ROUNDS)
                    variance = mean_var[:, 1:2]
                else:
                    act.wait_ge(var_ready, g + 1)
                    variance = var[:, g:g + 1]
                act.activation(std[:, g:g + 1], variance, ACT.Sqrt,
                               bias=eps_z2[:, g:g + 1]).then_inc(std_ready, 1)

            for g in range(LAST_ROUND):
                deviation(g)
            square_z(LAST_ROUND)
            copy_partial(LAST - 1, (LAST - 1) % SLOTS)
            deviation(LAST_ROUND)

        @block.tensor
        def _(pe):
            pe.wait_ge(consts_made, 4)
            pe.wait_ge(len_exp_ready, 1)
            pe.matmul(len_ps[:, 0:TILES], len_exp[:, :, :].rearrange("t b s -> t (b s)"),
                      ident[0:TILES, 0:TILES], start=True, stop=True).then_inc(len_p_ready, 1)

            def weighted_sums(t, s, dve_rows=0):
                half, b = s % 2, s % BUFS
                operands = [(weights[:, b, j, :], xs[s][:, j, :]) for j in range(ROWS - dve_rows)]
                if dve_rows:
                    operands += [(sel[:, (1 - half) * TB:(3 - half) * TB], row_sums[:, k, :]) for k in range(2)]
                total = 2 * ROWS if not dve_rows else ROWS + len(operands)
                for n, (stationary, moving) in enumerate(operands):
                    for k, (first, _) in enumerate(halves(ROWS - dve_rows)):
                        if n == first:
                            pe.wait_ge(weights_ready, 2 * t + k + 1)
                    m = half * ROWS + n
                    q = m % GROUPS
                    if dve_rows and n == ROWS - dve_rows:
                        pe.wait_ge(row_added, dve_rows)
                    done = pe.matmul(partial_ps[(s // 2) % 2][PB * q:PB * (q + 1), 0:D], stationary, moving,
                                     start=(m < GROUPS), stop=(m >= total - GROUPS))
                done.then_inc(tiles_summed, 1)

            def sum_z(s):
                rows, b = slice(PB * (s // 2), PB * (s // 2 + 1)), s % BUFS
                pe.matmul(z_ps[rows, 0:1], sel[:, TB:3 * TB], seg_sum[:, b:b + 1], start=True, stop=False)
                pe.matmul(z_ps[rows, 0:1], sel[:, 0:2 * TB], seg_sum[:, b + 1:b + 2],
                          start=False, stop=True).then_inc(z_summed, 1)

            def fold_groups(pair, s):
                rows, par = slice(PB * (s // 2), PB * (s // 2 + 1)), (s // 2) % 2
                pe.wait_ge(partial_copied, pair + 1)
                pe.matmul(raw_ps[rows, 0:D], fold[:, :], partial[:, par, :],
                          start=True, stop=True).then_inc(raw_summed, 1)

            def step(g, s, back):
                if back(1):
                    weighted_sums(*back(1))
                if s % 2 == 0 and back(2):
                    if s == 2 and back(SLOTS):
                        pe.wait_ge(eps_z2_ready, g)
                    sum_z(back(2)[1])
                if s % 2 == 1 and back(3):
                    if s == 3 and back(SLOTS):
                        pe.wait_ge(raw_copied, g)
                    fold_groups(GROUPS * g + (s - 3) // 2, back(3)[1])

            each_step(step, pe)
            pe.wait_ge(probs_ready, TILES)
            sum_z((LAST - 1) % SLOTS)
            weighted_sums(LAST, LAST % SLOTS, DVE_SUMS)
            fold_groups(TILES // 2 - 1, (LAST - 1) % SLOTS)

        @block.vector
        def _(dve):
            dve.wait_ge(len_landed, 16)
            dve.wait_ge(consts_made, 4)
            dve.tensor_copy(len_f[:, :], len_i[:, :]).then_inc(setup_step, 1)
            dve.tensor_reduce(fold[:, :], ident[:, :].rearrange("p (q c) -> p c q", q=GROUPS), AX_X,
                              ALU.add).then_inc(setup_step, 1)
            dve.wait_ge(setup_step, 2)
            dve.tensor_tensor(len_end[:, :], len_f[:, :], len_off[:, :], ALU.add).then_inc(setup_step, 1)
            dve.wait_ge(setup_step, 3)
            dve.tensor_copy(len_exp[:, :, :],
                            len_end[:, :].unsqueeze(2).to_broadcast([TILES, TB, SEGS])).then_inc(len_exp_ready, 1)
            dve.wait_ge(len_p_ready, 1)
            dve.tensor_copy(len_p[:, :], len_ps[:, 0:TILES]).then_inc(setup_step, 1)
            dve.wait_ge(setup_step, 4)
            dve.tensor_tensor(is_pad[:, :, :], pos[:, :].unsqueeze(1).to_broadcast([P, TILES, ROWS]),
                              len_p[:, :].unsqueeze(2).to_broadcast([P, TILES, ROWS]),
                              ALU.is_ge).then_inc(setup_step, 1)
            dve.wait_ge(setup_step, 5)
            dve.wait_ge(b_landed, 16)
            dve.tensor_scalar(penalty[:, :, :], is_pad[:, :, :], MASKED, b_rep[:, 0:1],
                              ALU.mult, ALU.add).then_inc(setup_step, 1)
            dve.wait_ge(setup_step, 6)
            dve.wait_ge(zeros_written, 2)
            dve.wait_ge(w_ps_ready, 1)

            def score_rows(g, s, lo, hi):
                for i, j in list(enumerate(DVE_ROWS))[lo:hi]:
                    if j in dve_load:
                        dve.wait_ge(x_landed[s][dve_load[j]], 16 * (g + 1))
                    done = dve.tensor_tensor_reduce(dve_prods[:, s % 2, i, :], xs[s][:, j, :],
                                                    w_ps[:, 0:D], 1.0, 0.0, ALU.mult, ALU.add,
                                                    scores[:, s % BUFS, j:j + 1])
                    if j == DVE_ROWS[-1]:
                        done.then_inc(dve_scores, 1)

            def mask(t, s):
                b = s % BUFS
                dve.wait_ge(dve_scores, t + 1)
                dve.wait_ge(act_scores, t + 1)
                dve.tensor_tensor(masked[:, b:b + 1, :], scores[:, b:b + 1, :], penalty[:, bass.ds(t, 1), :],
                                  ALU.add).then_inc(masked_ready, 1)

            def segment_max(t, s):
                b = s % BUFS
                dve.wait_ge(masked_ready, t + 1)
                dve.tensor_reduce(seg_max[:, b, 0:1], masked[:, b, :], AX_X, ALU.max).then_inc(seg_max_ready, 1)

            def turn(t, s):
                b = s % BUFS
                dve.wait_ge(seg_max_ready, t + 1)
                dve.transpose(turned[:, b, :], seg_max[:, b, :]).then_inc(turned_ready, 1)

            def across_segments(t, s):
                b = s % BUFS
                dve.wait_ge(turned_ready, t + 1)
                dve.tensor_reduce(batch_max[:, b, :], turned[:, b, :].rearrange("p (b s) -> p b s", s=SEGS),
                                  AX_X, ALU.max).then_inc(batch_max_ready, 1)

            def negate_and_spread(t, s):
                b = s % BUFS
                dve.wait_ge(batch_max_ready, t + 1)
                dve.tensor_scalar(spread_max[:, b, :].rearrange("p (b s) -> p b s", s=SEGS),
                                  batch_max[:, b, :].unsqueeze(2).to_broadcast([P, QUAD // SEGS, SEGS]),
                                  -1.0, None, ALU.mult).then_inc(spread_max_ready, 1)

            def turn_back(t, s):
                b = s % BUFS
                dve.wait_ge(spread_max_ready, t + 1)
                dve.transpose(neg_max[:, b, :], spread_max[:, b, :]).then_inc(neg_max_ready, 1)

            CHAIN = (mask, segment_max, turn, across_segments, negate_and_spread, turn_back)

            def of_round(buf, g):
                return buf[:, bass.ds(g, 1), :].rearrange("p o d -> p (o d)")

            def keep_var(g):
                dve.tensor_copy(var[:, bass.ds(g, 1)], mean_var[:, 1:2]).then_inc(var_ready, 1)

            def moments():
                dve.bn_aggr(mean_var[:, :], stats[:, :]).then_inc(mean_var_ready, 1)

            def centre(g, r):
                dve.scalar_tensor_tensor(of_round(scaled, g), r, mean_var[:, 0:1], gamma_rep[:, :],
                                         ALU.subtract, ALU.mult).then_inc(scaled_ready, 1)

            def reciprocals(lo, hi):
                dve.wait_ge(std_ready, hi)
                dve.reciprocal(rstd[:, lo:hi], std[:, lo:hi]).then_inc(rstd_ready, 1)

            def normalise(g):
                dve.wait_ge(rstd_ready, 1 if g < LAST_ROUND else 2)
                dve.wait_ge(scaled_ready, g + 1)
                dve.scalar_tensor_tensor(result[:, g, :], scaled[:, g, :], rstd[:, g:g + 1], beta_rep[:, :],
                                         ALU.mult, ALU.add).then_inc(result_ready, 1)

            def add_row(n, s):
                j, into = ROWS - DVE_SUMS + n, row_sums[:, n % 2, :]
                prob = probs[:, s % BUFS, j:j + 1]
                if n < 2:
                    done = dve.tensor_scalar(into, xs[s][:, j, :], prob, None, ALU.mult)
                else:
                    dve.wait_ge(row_added, n - 1)
                    done = dve.scalar_tensor_tensor(into, xs[s][:, j, :], prob, into, ALU.mult, ALU.add)
                done.then_inc(row_added, 1)

            def step(g, s, back):
                for n, link in enumerate(CHAIN):
                    if back(1):
                        link(*back(1))
                    if n == 0 and back(2):
                        dve.wait_ge(dve_scores, back(2)[0] + 1)
                    score_rows(g, s, n, n + 1)
                score_rows(g, s, len(CHAIN), len(DVE_ROWS) - 1)
                if back(SLOTS):
                    if s == 2:
                        dve.wait_ge(raw_summed, GROUPS * g)
                    if s == 3:
                        dve.wait_ge(stats_ready, g)
                    if s == 4:
                        dve.wait_ge(mean_var_ready, g)
                        dve.wait_ge(raw_copied, g)
                        dve.wait_ge(gamma_landed, 16)
                    if s == 5:
                        dve.wait_ge(var_ready, g)
                        dve.wait_ge(scaled_ready, g)
                score_rows(g, s, len(DVE_ROWS) - 1, len(DVE_ROWS))
                if s == 2 and back(SLOTS):
                    dve.bn_stats(stats[:, :], raw_ps[:, 0:D]).then_inc(stats_ready, 1)
                    dve.tensor_copy(of_round(raw, g - 1), raw_ps[:, 0:D]).then_inc(raw_copied, 1)
                if s == 3 and back(SLOTS):
                    moments()
                if s == 4 and back(SLOTS):
                    keep_var(g - 1)
                    centre(g - 1, of_round(raw, g - 1))

            each_step(step, dve)
            for link in CHAIN:
                link(LAST, LAST % SLOTS)
            dve.wait_ge(probs_ready, TILES)
            for n in range(DVE_SUMS):
                add_row(n, LAST % SLOTS)

            dve.wait_ge(beta_landed, 16)
            reciprocals(0, LAST_ROUND)
            for g in range(LAST_ROUND):
                normalise(g)
            g = LAST_ROUND
            dve.wait_ge(raw_summed, TILES // 2)
            dve.bn_stats(stats[:, :], raw_ps[:, 0:D]).then_inc(stats_ready, 1)
            dve.wait_ge(stats_ready, ROUNDS)
            moments()
            dve.wait_ge(mean_var_ready, ROUNDS)
            centre(g, raw_ps[:, 0:D])
            reciprocals(g, ROUNDS)
            normalise(g)


_INS = ['r_padded_embeddings', 'r_lengths', 'L0_rec_w_att', 'L0_rec_b_att', 'L0_rec_ln_gamma', 'L0_rec_ln_beta']


def kernel(**inputs):
    import numpy as _np
    import concourse.bacc as _bacc
    from concourse import mybir as _mybir
    from concourse.bass_utils import run_bass_kernel_spmd as _run

    nc = _bacc.Bacc("TRN2", target_bir_lowering=False, num_devices=1)
    arrays, args = {}, []
    for name in _INS:
        a = _np.ascontiguousarray(inputs[name])
        arrays[f"in_{name}_dram"] = a
        args.append(nc.dram_tensor(f"in_{name}_dram", a.shape, _mybir.dt.from_np(a.dtype), kind="ExternalInput").ap())
    B, _, D = inputs['r_padded_embeddings'].shape
    args.append(nc.dram_tensor("out_dram", (B, D), _mybir.dt.float32, kind="ExternalOutput").ap())
    attention_pool_layernorm(nc, *args)
    r = _run(nc, [arrays], core_ids=[0])
    return r.results[0]["out_dram"]
```
